# Optimizing a Trainium2 kernel written in Bass

```python
import numpy as np
import jax
import jax.numpy as jnp

def _softmax(x, axis=-1):
    return jax.nn.softmax(x, axis=axis)

def _gelu(x):
    return jax.nn.gelu(x, approximate=True)

def _silu(x):
    return jax.nn.silu(x)

def _sigmoid(x):
    return jax.nn.sigmoid(x)

def _layernorm(x, axis=-1, eps=1e-05):
    m = jnp.mean(x, axis=axis, keepdims=True)
    v = jnp.var(x, axis=axis, keepdims=True)
    return (x - m) / jnp.sqrt(v + eps)

def _scatter_add(tgt, idx, src, axis=0):
    return tgt.at[idx].add(src)

def _segment_sum(src, seg, n):
    return jax.ops.segment_sum(src, seg, n)
kernel_name = 'mk_rec_standalone_d1_rec_r8_d2d4fa'

def setup_inputs(seed: int=0):
    np.random.seed(seed)
    _w = jnp.asarray

    def _rec_inputs():
        import jax
        import jax.numpy as jnp
        _rk = jax.random.key(seed)
        r_x = -0.000292821 + 1.00034 * jax.random.normal(jax.random.fold_in(_rk, 1), (512, 64, 64), jnp.float32)
        return r_x
    r_x = _rec_inputs()

    def _L0_rec_setup():
        import jax, jax.numpy as jnp
        import numpy as np
        B, F, D = (1024, 64, 64)
        key = jax.random.key(seed)
        ks = jax.random.split(key, 7)
        return {'x': jax.random.normal(ks[0], (B, F, D), dtype=jnp.float32), 'W1': jax.random.normal(ks[1], (F, F * F), dtype=jnp.float32) * 0.02, 'b1': jax.random.normal(ks[2], (F,), dtype=jnp.float32) * 0.02, 'W2': jax.random.normal(ks[3], (F, F * F), dtype=jnp.float32) * 0.02, 'b2': jax.random.normal(ks[4], (F,), dtype=jnp.float32) * 0.02, 'Wfc': jax.random.normal(ks[5], (1, 2 * F), dtype=jnp.float32) * 0.02, 'bfc': jax.random.normal(ks[6], (1,), dtype=jnp.float32) * 0.02}
    _L0_rec_all = _L0_rec_setup()
    _L0_rec_in = {k: v for k, v in _L0_rec_all.items() if k in ('W1', 'b1', 'W2', 'b2', 'Wfc', 'bfc')}
    del _L0_rec_all
    return {'r_x': r_x, 'L0_rec_W1': _L0_rec_in['W1'], 'L0_rec_b1': _L0_rec_in['b1'], 'L0_rec_W2': _L0_rec_in['W2'], 'L0_rec_b2': _L0_rec_in['b2'], 'L0_rec_Wfc': _L0_rec_in['Wfc'], 'L0_rec_bfc': _L0_rec_in['bfc']}

def reference(r_x, L0_rec_W1, L0_rec_b1, L0_rec_W2, L0_rec_b2, L0_rec_Wfc, L0_rec_bfc):
    import jax
    import jax.numpy as jnp

    def _L0_rec_ref(x, W1, b1, W2, b2, Wfc, bfc):
        import jax, jax.numpy as jnp
        import numpy as np
        B, F, D = (1024, 64, 64)
        b_, f0, d = x.shape
        x0 = x[:, :, None, :]
        h = x
        xs = []
        for W, b in ((W1, b1), (W2, b2)):
            z = (x0 * h[:, None, :, :]).reshape(b_, f0 * f0, d)
            h = jax.nn.relu(jnp.einsum('oc,bcd->bod', W, z) + b[None, :, None])
            xs.append(h)
        pooled = jnp.sum(jnp.concatenate(xs, axis=1), axis=2)
        return pooled @ Wfc.T + bfc
    y = _L0_rec_ref(r_x, L0_rec_W1, L0_rec_b1, L0_rec_W2, L0_rec_b2, L0_rec_Wfc, L0_rec_bfc)
    return y

_drawn_inputs = setup_inputs


def setup_inputs(seed=0):
    import zlib

    import numpy as np

    out = dict(_drawn_inputs(seed))
    spreads = {}
    factors = {'L0_rec_b2': 4.598}
    for name, (base, spread) in spreads.items():
        noise = np.random.default_rng([zlib.crc32(name.encode()), seed]).standard_normal(out[name].shape)
        drawn = base * np.exp(spread * noise) if base else spread * noise
        out[name] = jnp.asarray(drawn.astype(out[name].dtype))
    for name, factor in factors.items():
        out[name] = (out[name] * factor).astype(out[name].dtype)
    return out
```

```python
from contextlib import ExitStack

import numpy as np
import concourse.bass as bass
from concourse import mybir

ALU = mybir.AluOpType
ACT = mybir.ActivationFunctionType
F32 = mybir.dt.float32

P = 128
FEAT = 64
EMB = 64
BATCH = 512
TILE_B = 8
T = TILE_B * EMB
HALVES = 2
PAIRS = BATCH // (TILE_B * HALVES)
BLK = 4
NBLK = FEAT // BLK
MATCH = NBLK - 1
MAIN = MATCH * (NBLK // 2 - 1)
SPARE = MATCH * (NBLK // 2)
NSPARE = P - SPARE
SLOTS = 2 * BLK
DIAG = FEAT + FEAT // 2
C1 = BLK * BLK
C2 = SLOTS * BLK

KS = NBLK // 2 - 1
ORDER = [MATCH] + 2 * list(range(MATCH))
ORDER = ORDER[:1 + MATCH + 2 * KS]
XROWS = len(ORDER) * BLK
HROWS = (1 + MATCH + KS) * BLK

DVE_B = 3
V_RING = 3
G_RING = 2
DMA = 16


def partition_features():
    feats = np.zeros((P, SLOTS), np.int64)
    hblk = np.zeros(P, np.int64)
    four = np.arange(BLK)
    for n in range(MATCH):
        for k in range(1, KS + 1):
            p = n * KS + k - 1
            feats[p] = np.concatenate([(n + 2 * k) % MATCH * BLK + four, n * BLK + four])
            hblk[p] = (n + k) % MATCH
        feats[MAIN + n] = np.concatenate([MATCH * BLK + four, n * BLK + four])
        hblk[MAIN + n] = n
    for s in range(NSPARE):
        one, two = ORDER[s] * BLK, ORDER[s + NSPARE] * BLK
        feats[SPARE + s] = [one, one + 1, two, two + 1, one + 2, one + 3, two + 2, two + 3]
        hblk[SPARE + s] = MATCH
    return feats, hblk


def feature_order():
    return np.array([ORDER[r // BLK] * BLK + r % BLK for r in range(FEAT)])


def build(nc, x, w1, w1t, w2, bias, wfc, bfc, out):
    with ExitStack() as ctx:
        def sb(name, shape):
            return ctx.enter_context(nc.sbuf_tensor(name, shape, F32))

        def sem(name):
            return ctx.enter_context(nc.semaphore(name))

        xs = sb("xs", [P, 2, HALVES, SLOTS, T])
        hrep = sb("hrep", [P, HALVES, BLK, T])
        diag0 = sb("diag0", [DIAG, HALVES, T])
        diag1 = sb("diag1", [DIAG, HALVES, T])
        zv = sb("zv", [P, V_RING, HALVES, BLK, T])
        zg = sb("zg", [P, G_RING, HALVES, BLK, T])
        zd = sb("zd", [DIAG, HALVES, T])
        w1s = sb("w1s", [P, C1 + 1, FEAT])
        w2s = sb("w2s", [P, C2, FEAT])
        bias_s = sb("bias_s", [P, 2])
        wfc_s = sb("wfc_s", [P, 2, HALVES])
        bfc_s = sb("bfc_s", [HALVES, 1])
        h1 = sb("h1", [P, T])
        h2 = sb("h2", [P, T])
        pooled = sb("pooled", [P, 2, PAIRS, TILE_B])
        out_s = sb("out_s", [HALVES, PAIRS * TILE_B])
        w1t_s = zg[:, 0, 0].rearrange("p b t -> p (b t)")[:, 0:(C1 + 1) * FEAT].rearrange(
            "p (c o) -> p c o", o=FEAT)

        operand = [[ctx.enter_context(nc.psum_tensor(f"operand{b}{h}", [P, T], F32))
                    for h in range(HALVES)] for b in range(DVE_B)]
        acc1 = ctx.enter_context(nc.psum_tensor("acc1", [P, T], F32))
        acc2 = ctx.enter_context(nc.psum_tensor("acc2", [P, T], F32))

        h_dram = nc.dram_tensor("h_scratch", [2, HALVES * HROWS, T], F32, kind="Internal").ap()

        weights_loaded = sem("weights_loaded")
        w1_summed = sem("w1_summed")
        xa_loaded = [sem(f"xa_loaded{i}") for i in range(2)]
        xb_loaded = [sem(f"xb_loaded{i}") for i in range(2)]
        diag_loaded = sem("diag_loaded")
        operand_ready = sem("operand_ready")
        zv_ready = sem("zv_ready")
        zg_ready = sem("zg_ready")
        zd_ready = sem("zd_ready")
        zv_used = sem("zv_used")
        zg_used = sem("zg_used")
        zd_used = sem("zd_used")
        acc2_copied = sem("acc2_copied")
        h1_ready = sem("h1_ready")
        h2_ready = sem("h2_ready")
        h1_stored = sem("h1_stored")
        h_loaded = sem("h_loaded")
        final_ready = sem("final_ready")
        out_ready = sem("out_ready")
        out_stored = sem("out_stored")

        X_DMAS, DIAG_DMAS, STORE_DMAS, H_DMAS, W_DMAS = 5, 4, 4, 4, 6

        def v_units(phase, b):
            return phase * DVE_B + (b + 1)

        def halves(phase, b, h):
            return phase * (DVE_B * HALVES) + (b * HALVES + h + 1)

        def steps(eng, step):
            step(0, 0, 1)
            with eng.Fori(0, PAIRS // 2 - 2) as j:
                step(j * 2 + 1, 1, j + 2)
                step(j * 2 + 2, 0, j + 2)
            for s in range(PAIRS - 3, PAIRS):
                step(s, s % 2, (s + 1) // 2 + 1)

        def is_last(s):
            return isinstance(s, int) and s == PAIRS - 1

        def last_phase(s):
            return s * 3 + (2 if is_last(s) else 3)

        block = ctx.enter_context(nc.Block())

        @block.sync
        def _(sp):
            def rows(tensor, index, row, dims, run=BLK):
                whole = tensor[index]
                return bass.AP(tensor=whole.tensor, offset=whole.offset + row * T,
                               ap=[[step * T, n] for step, n in dims] + [[1, run * T]])

            def load_x(g, parity, part):
                loaded = (xa_loaded, xb_loaded)[part][parity]
                dst = xs[:, parity, :, part * BLK:(part + 1) * BLK, :]
                k_step = 2 * BLK if part == 0 else 0
                for h in range(HALVES):
                    sp.dma_start(dst[0:MAIN, h].rearrange("p a t -> p (a t)"),
                                 rows(x, g, h * XROWS + BLK + k_step,
                                      [[BLK, MATCH], [k_step, KS]])).then_inc(loaded, DMA)
                    two = BLK // 2
                    sp.dma_start(dst[SPARE:P, h].rearrange("p (v f) t -> p v (f t)", v=2),
                                 rows(x, g, h * XROWS + part * two,
                                      [[BLK, NSPARE], [NSPARE * BLK, 2]], two)
                                 ).then_inc(loaded, DMA)
                row, step = (0, 0) if part == 0 else (BLK, BLK)
                sp.dma_start(dst[MAIN:SPARE].rearrange("p h a t -> p h (a t)"),
                             rows(x, g, row, [[step, MATCH], [XROWS, HALVES]])
                             ).then_inc(loaded, DMA)

            def load_diag(g):
                xg = x[g]
                for dst, odd in ((diag0, 0), (diag1, 1)):
                    sp.dma_start(dst[0:FEAT], xg[:, 0:FEAT, :].rearrange("h r t -> r h t")
                                 ).then_inc(diag_loaded, DMA)
                    sp.dma_start(dst[FEAT:DIAG], xg[:, odd:FEAT:2, :].rearrange("h r t -> r h t")
                                 ).then_inc(diag_loaded, DMA)

            def spread_h1(g, parity):
                sp.wait_ge(h1_ready, g + 1)
                for h in range(HALVES):
                    sp.dma_start(h_dram[parity, h * HROWS:h * HROWS + FEAT, :], h1[h * FEAT:(h + 1) * FEAT, :]
                                 ).then_inc(h1_stored, DMA)
                    sp.dma_start(h_dram[parity, h * HROWS + FEAT:(h + 1) * HROWS, :],
                                 h1[h * FEAT + BLK:h * FEAT + BLK + KS * BLK, :]
                                 ).then_inc(h1_stored, DMA)

            def load_h(g, parity, stored):
                sp.wait_ge(h1_stored, stored)
                dst = hrep[:, :, :, :].rearrange("p h b t -> p h (b t)")
                for h in range(HALVES):
                    sp.dma_start(dst[0:MAIN, h], rows(h_dram, parity, h * HROWS + 2 * BLK,
                                                      [[BLK, MATCH], [BLK, KS]])
                                 ).then_inc(h_loaded, DMA)
                sp.dma_start(dst[MAIN:SPARE], rows(h_dram, parity, BLK,
                                                   [[BLK, MATCH], [HROWS, HALVES]])
                             ).then_inc(h_loaded, DMA)
                sp.dma_start(dst[SPARE:P], rows(h_dram, parity, 0, [[0, NSPARE], [HROWS, HALVES]])
                             ).then_inc(h_loaded, DMA)

            sp.dma_start(w1s[:, :, :], w1).then_inc(weights_loaded, DMA)
            sp.dma_start(w1t_s, w1t).then_inc(weights_loaded, DMA)
            load_x(0, 0, 1)
            load_x(0, 0, 0)
            load_diag(0)
            sp.dma_start(w2s[:, :, :], w2).then_inc(weights_loaded, DMA)
            sp.dma_start(bias_s[:, :], bias).then_inc(weights_loaded, DMA)
            sp.dma_start(wfc_s[:, :, :], wfc).then_inc(weights_loaded, DMA)
            sp.dma_start(bfc_s[:, :], bfc).then_inc(weights_loaded, DMA)
            load_x(1, 1, 1)
            load_x(1, 1, 0)
            sp.wait_ge(zd_ready, 1)
            load_diag(1)
            spread_h1(0, 0)
            load_h(0, 0, STORE_DMAS * DMA)

            def value(v):
                if not isinstance(v, int):
                    sp.compute_val(v)
                return v

            def step(s, parity, nth):
                if is_last(s):
                    return
                phase_done = value(halves(s * 3 + 1, DVE_B - 1, 1))
                g_phase_done = value(s * 6 + 4)
                phases_done = value(halves(s * 3 + 3, DVE_B - 1, 1))
                g_phases_done = value(s * 6 + 8)
                stored = value((s + 2) * (STORE_DMAS * DMA))
                more = not (isinstance(s, int) and s + 2 >= PAIRS)
                if more:
                    sp.wait_ge(zd_ready, s + 2)
                    load_diag(s + 2)
                    sp.wait_ge(zv_ready, phase_done)
                    sp.wait_ge(zg_ready, g_phase_done)
                    load_x(s + 2, parity, 0)
                spread_h1(s + 1, 1 - parity)
                sp.wait_ge(operand_ready, phases_done)
                sp.wait_ge(zg_ready, g_phases_done)
                load_h(s + 1, 1 - parity, stored)
                if more:
                    sp.wait_ge(zv_ready, phases_done)
                    load_x(s + 2, parity, 1)

            steps(sp, step)
            sp.wait_ge(out_ready, 1)
            sp.dma_start(out, out_s[:, :].rearrange("h (g b) -> h g b", b=TILE_B)
                         ).then_inc(out_stored, DMA)
            sp.wait_ge(out_stored, DMA)

        @block.scalar
        def _(act):
            def fill(phase, source):
                for b in range(DVE_B):
                    for h in range(HALVES):
                        if not (isinstance(phase, int) and phase == 0):
                            act.wait_ge(zv_ready, halves(phase - 1, b, h))
                        act.copy(operand[b][h][:, :], source(b, h)).then_inc(operand_ready, 1)

            def relu_and_pool(layer, g, source, dest, done):
                for b in range(TILE_B):
                    cols = slice(b * EMB, (b + 1) * EMB)
                    last = act.activation(dest[:, cols], source[:, cols], ACT.Relu,
                                          bias=bias_s[:, layer:layer + 1],
                                          accum_out=pooled[:, layer, g, b:b + 1])
                last.then_inc(done, 1)

            def layer1_end(g, phase):
                act.wait_ge(zv_used, v_units(phase, DVE_B - 1))
                if not (isinstance(g, int) and g == 0):
                    act.wait_ge(h1_stored, g * (STORE_DMAS * DMA))
                relu_and_pool(0, g, acc1, h1, h1_ready)

            def layer2_end(phase):
                act.wait_ge(zv_used, v_units(phase, DVE_B - 1))
                act.copy(h2[:, :], acc2[:, :]).then_inc(acc2_copied, 1)

            def layer2_pool(g):
                act.wait_ge(acc2_copied, g + 1)
                relu_and_pool(1, g, h2, h2, h2_ready)

            act.wait_ge(xb_loaded[0], X_DMAS * DMA)
            fill(0, lambda b, h: xs[:, 0, h, BLK + b, :])
            act.wait_ge(weights_loaded, W_DMAS * DMA)
            layer1_end(0, 0)

            def step(s, parity, nth):
                act.wait_ge(h_loaded, (s + 1) * (H_DMAS * DMA))
                fill(s * 3 + 1, lambda b, h: hrep[:, h, b, :])
                first = isinstance(s, int) and s == 0
                if not first:
                    layer2_end(s * 3)
                if not is_last(s):
                    act.wait_ge(xb_loaded[1 - parity], nth * (X_DMAS * DMA))
                    fill(s * 3 + 2, lambda b, h: xs[:, 1 - parity, h, BLK + b, :])
                if not first:
                    layer2_pool(s - 1)
                fill(last_phase(s), lambda b, h: hrep[:, h, b, :])
                if not is_last(s):
                    layer1_end(s + 1, s * 3 + 2)

            steps(act, step)
            layer2_end(last_phase(PAIRS - 1))
            layer2_pool(PAIRS - 1)
            act.wait_ge(final_ready, 1)
            act.activation(out_s[:, :], acc1[0:HALVES, 0:PAIRS * TILE_B], ACT.Identity,
                           bias=bfc_s[:, :]).then_inc(out_ready, 1)

        @block.vector
        def _(dve):
            def products(phase, parity, part):
                for b in range(DVE_B):
                    if not (isinstance(phase, int) and phase == 0):
                        dve.wait_ge(zv_used, v_units(phase - 1, b))
                    for h in range(HALVES):
                        dve.wait_ge(operand_ready, halves(phase, b, h))
                        dve.tensor_tensor(
                            zv[:, b, h, :, :], xs[:, parity, h, part * BLK:(part + 1) * BLK, :],
                            operand[b][h][:, :].unsqueeze(1).broadcast_to((P, BLK, T)),
                            ALU.mult).then_inc(zv_ready, 1)

            dve.wait_ge(xa_loaded[0], X_DMAS * DMA)
            products(0, 0, 0)
            dve.wait_ge(weights_loaded, W_DMAS * DMA)
            dve.tensor_tensor(w1s[:, :, :], w1s[:, :, :], w1t_s, ALU.add).then_inc(w1_summed, 1)

            def step(s, parity, nth):
                products(s * 3 + 1, parity, 0)
                if not is_last(s):
                    dve.wait_ge(xa_loaded[1 - parity], nth * (X_DMAS * DMA))
                    products(s * 3 + 2, 1 - parity, 0)
                products(last_phase(s), parity, 1)

            steps(dve, step)

        @block.gpsimd
        def _(pool):
            def products(phase, phase_parity, parity, part, value):
                if not (isinstance(phase, int) and phase < G_RING):
                    pool.wait_ge(zg_used, phase - (G_RING - 1))
                for h in range(HALVES):
                    pool.tensor_tensor(
                        zg[:, phase_parity, h, :, :], xs[:, parity, h, part * BLK:(part + 1) * BLK, :],
                        value(h).unsqueeze(1).broadcast_to((P, BLK, T)), ALU.mult
                    ).then_inc(zg_ready, 1)

            def diagonal(g):
                pool.wait_ge(diag_loaded, (g + 1) * (DIAG_DMAS * DMA))
                if not (isinstance(g, int) and g == 0):
                    pool.wait_ge(zd_used, g)
                pool.tensor_tensor(zd[:, :, :], diag0[:, :, :], diag1[:, :, :], ALU.mult
                                   ).then_inc(zd_ready, 1)

            pool.wait_ge(xa_loaded[0], X_DMAS * DMA)
            pool.wait_ge(xb_loaded[0], X_DMAS * DMA)
            diagonal(0)
            pool.wait_ge(w1_summed, 1)
            products(0, 0, 0, 0, lambda h: xs[:, 0, h, SLOTS - 1, :])
            diagonal(1)

            def step(s, parity, nth):
                pool.wait_ge(h_loaded, (s + 1) * (H_DMAS * DMA))
                products(s * 3 + 1, (1 + parity) % 2, parity, 0, lambda h: hrep[:, h, BLK - 1, :])
                if not is_last(s):
                    pool.wait_ge(xa_loaded[1 - parity], nth * (X_DMAS * DMA))
                    pool.wait_ge(xb_loaded[1 - parity], nth * (X_DMAS * DMA))
                    products(s * 3 + 2, parity, 1 - parity, 0,
                             lambda h: xs[:, 1 - parity, h, SLOTS - 1, :])
                    if not (isinstance(s, int) and s + 2 >= PAIRS):
                        diagonal(s + 2)
                products(last_phase(s), parity if is_last(s) else (1 + parity) % 2, parity, 1,
                         lambda h: hrep[:, h, BLK - 1, :])

            steps(pool, step)

        @block.tensor
        def _(pe):
            def chunk(acc, weights, z, first, last):
                rows = z(0).shape[0]
                for h in range(HALVES):
                    mm = pe.matmul(acc[h * FEAT:(h + 1) * FEAT, :], weights[0:rows], z(h),
                                   start=first, stop=last)
                return mm

            def unit(acc, weights, z, first, last):
                for a in range(BLK):
                    mm = chunk(acc, weights[:, a], lambda h: z[:, h, a, :],
                               first and a == 0, last and a == BLK - 1)
                return mm

            def phase_sum(phase, phase_parity, acc, weights, opens, closes):
                for turn, b in enumerate((0, 1, BLK - 1, DVE_B - 1)):
                    first, last = opens and turn == 0, closes and turn == BLK - 1
                    w = weights[:, b * BLK:(b + 1) * BLK]
                    if b < DVE_B:
                        pe.wait_ge(zv_ready, halves(phase, b, 1))
                        mm = unit(acc, w, zv[:, b], first, last)
                        mm.then_inc(zv_used, 1)
                    else:
                        pe.wait_ge(zg_ready, phase * HALVES + HALVES)
                        mm = unit(acc, w, zg[:, phase_parity], first, last)
                        mm.then_inc(zg_used, 1)

            def diagonal(g):
                pe.wait_ge(zd_ready, g + 1)
                if not (isinstance(g, int) and g == 0):
                    pe.wait_ge(h1_ready, g)
                chunk(acc1, w1s[0:DIAG, C1], lambda h: zd[:, h, :], True, False
                      ).then_inc(zd_used, 1)

            pe.wait_ge(weights_loaded, W_DMAS * DMA)
            pe.wait_ge(w1_summed, 1)
            diagonal(0)
            phase_sum(0, 0, acc1, w1s, False, True)

            def step(s, parity, nth):
                if not is_last(s):
                    diagonal(s + 1)
                if not (isinstance(s, int) and s == 0):
                    pe.wait_ge(acc2_copied, s)
                phase_sum(s * 3 + 1, (1 + parity) % 2, acc2, w2s[:, 0:C1], True, False)
                if not is_last(s):
                    phase_sum(s * 3 + 2, parity, acc1, w1s, False, True)
                phase_sum(last_phase(s), parity if is_last(s) else (1 + parity) % 2,
                          acc2, w2s[:, C1:C2], False, True)

            steps(pe, step)
            pe.wait_ge(h1_ready, PAIRS)
            pe.wait_ge(h2_ready, PAIRS)
            for layer in range(2):
                mm = pe.matmul(acc1[0:HALVES, 0:PAIRS * TILE_B], wfc_s[:, layer, :],
                               pooled[:, layer, :, :].rearrange("p g b -> p (g b)"),
                               start=(layer == 0), stop=(layer == 1))
            mm.then_inc(final_ready, 1)


def lay_out(r_x, W1, b1, W2, b2, Wfc, bfc):
    feats, hblk = partition_features()
    order = feature_order()
    tiles = r_x.reshape(PAIRS, HALVES, TILE_B, FEAT, EMB).transpose(0, 1, 3, 2, 4)
    tiles = tiles.reshape(PAIRS, HALVES, NBLK, BLK, T)
    x = tiles[:, :, ORDER].reshape(PAIRS, HALVES, XROWS, T)

    W1 = W1.reshape(FEAT, FEAT, FEAT)[order]
    W2 = W2.reshape(FEAT, FEAT, FEAT)[order]
    w1 = np.zeros((P, C1 + 1, FEAT), W1.dtype)
    w1t = np.zeros_like(w1)
    for b in range(BLK):
        for a in range(BLK):
            i, j = feats[:, a], feats[:, BLK + b]
            use = (np.arange(P) < SPARE) | (i // BLK == j // BLK)
            c = b * BLK + a
            w1[use, c] = W1[:, i, j].T[use]
            w1t[use, c] = W1[:, j, i].T[use]
    i = np.concatenate([order, order[0::2]])
    j = np.concatenate([order, order[1::2]])
    w1[:DIAG, C1] = W1[:, i, j].T
    w1t[FEAT:DIAG, C1] = W1[:, j, i].T[FEAT:]
    w2 = np.zeros((P, C2, FEAT), W2.dtype)
    for s in range(SLOTS):
        for b in range(BLK):
            c = (s // BLK) * C1 + b * BLK + s % BLK
            w2[:, c] = W2[:, feats[:, s], hblk * BLK + b].T
    bias = np.tile(np.stack([b1[order], b2[order]], axis=1), (HALVES, 1))
    wfc = np.zeros((P, 2, HALVES), Wfc.dtype)
    for h in range(HALVES):
        wfc[h * FEAT:(h + 1) * FEAT, :, h] = Wfc[0].reshape(2, FEAT)[:, order].T
    return {"x": x, "w1": w1, "w1t": w1t, "w2": w2, "bias": bias, "wfc": wfc,
            "bfc": np.tile(bfc.reshape(1, 1), (HALVES, 1))}


def kernel(r_x, L0_rec_W1, L0_rec_b1, L0_rec_W2, L0_rec_b2, L0_rec_Wfc, L0_rec_bfc):
    import concourse.bacc as bacc
    from concourse.bass_utils import run_bass_kernel_spmd

    given = (r_x, L0_rec_W1, L0_rec_b1, L0_rec_W2, L0_rec_b2, L0_rec_Wfc, L0_rec_bfc)
    arrays = {n: np.ascontiguousarray(a) for n, a in lay_out(*map(np.asarray, given)).items()}
    nc = bacc.Bacc("TRN2", target_bir_lowering=False, num_devices=1)
    args = [nc.dram_tensor(n, a.shape, F32, kind="ExternalInput").ap() for n, a in arrays.items()]
    out = nc.dram_tensor("out", (BATCH, 1), F32, kind="ExternalOutput").ap()
    build(nc, *args, out.rearrange("(g h b) o -> h g (b o)", h=HALVES, b=TILE_B))
    result = run_bass_kernel_spmd(nc, [arrays], core_ids=[0])
    return result.results[0]["out"]
```

```python
from contextlib import ExitStack

import numpy as np
import concourse.bass as bass
from concourse import mybir

ALU = mybir.AluOpType
ACT = mybir.ActivationFunctionType
F32 = mybir.dt.float32

P = 128
FEAT = 64
EMB = 64
BATCH = 512
TILE_B = 8
T = TILE_B * EMB
HALVES = 2
PAIRS = BATCH // (TILE_B * HALVES)
BLK = 4
NBLK = FEAT // BLK
MATCH = NBLK - 1
MAIN = MATCH * (NBLK // 2 - 1)
SPARE = MATCH * (NBLK // 2)
NSPARE = P - SPARE
SLOTS = 2 * BLK
DIAG = FEAT + FEAT // 2
C1 = BLK * BLK
C2 = SLOTS * BLK

KS = NBLK // 2 - 1
ORDER = [MATCH] + 2 * list(range(MATCH))
ORDER = ORDER[:1 + MATCH + 2 * KS]
XROWS = len(ORDER) * BLK
HROWS = (1 + MATCH + KS) * BLK

DVE_B = 3
V_RING = 3
G_RING = 2
DMA = 16


def partition_features():
    feats = np.zeros((P, SLOTS), np.int64)
    hblk = np.zeros(P, np.int64)
    four = np.arange(BLK)
    for n in range(MATCH):
        for k in range(1, KS + 1):
            p = n * KS + k - 1
            feats[p] = np.concatenate([(n + 2 * k) % MATCH * BLK + four, n * BLK + four])
            hblk[p] = (n + k) % MATCH
        feats[MAIN + n] = np.concatenate([MATCH * BLK + four, n * BLK + four])
        hblk[MAIN + n] = n
    for s in range(NSPARE):
        one, two = ORDER[s] * BLK, ORDER[s + NSPARE] * BLK
        feats[SPARE + s] = [one, one + 1, two, two + 1, one + 2, one + 3, two + 2, two + 3]
        hblk[SPARE + s] = MATCH
    return feats, hblk


def feature_order():
    return np.array([ORDER[r // BLK] * BLK + r % BLK for r in range(FEAT)])


def build(nc, x, w1, w1t, w2, bias, wfc, bfc, out):
    with ExitStack() as ctx:
        def sb(name, shape):
            return ctx.enter_context(nc.sbuf_tensor(name, shape, F32))

        def sem(name):
            return ctx.enter_context(nc.semaphore(name))

        xs = sb("xs", [P, 2, HALVES, SLOTS, T])
        hrep = sb("hrep", [P, HALVES, BLK, T])
        diag0 = sb("diag0", [DIAG, HALVES, T])
        diag1 = sb("diag1", [DIAG, HALVES, T])
        zv = sb("zv", [P, V_RING, HALVES, BLK, T])
        zg = sb("zg", [P, G_RING, HALVES, BLK, T])
        zd = sb("zd", [DIAG, HALVES, T])
        w1s = sb("w1s", [P, C1 + 1, FEAT])
        w2s = sb("w2s", [P, C2, FEAT])
        bias_s = sb("bias_s", [P, 2])
        wfc_s = sb("wfc_s", [P, 2, HALVES])
        bfc_s = sb("bfc_s", [HALVES, 1])
        h1 = sb("h1", [P, T])
        h2 = sb("h2", [P, T])
        unread = sb("unread", [P, 2, T])
        pooled = sb("pooled", [P, 2, PAIRS, TILE_B])
        out_s = sb("out_s", [HALVES, PAIRS * TILE_B])
        w1t_s = zg[:, 0, 0].rearrange("p b t -> p (b t)")[:, 0:(C1 + 1) * FEAT].rearrange(
            "p (c o) -> p c o", o=FEAT)

        operand = [[ctx.enter_context(nc.psum_tensor(f"operand{b}{h}", [P, T], F32))
                    for h in range(HALVES)] for b in range(DVE_B)]
        acc1 = ctx.enter_context(nc.psum_tensor("acc1", [P, T], F32))
        acc2 = ctx.enter_context(nc.psum_tensor("acc2", [P, T], F32))

        h_dram = nc.dram_tensor("h_scratch", [2, HALVES * HROWS, T], F32, kind="Internal").ap()

        weights_loaded = sem("weights_loaded")
        w1_loaded = sem("w1_loaded")
        w1_summed = sem("w1_summed")
        xa_loaded = [sem(f"xa_loaded{i}") for i in range(2)]
        xb_loaded = [sem(f"xb_loaded{i}") for i in range(2)]
        diag_loaded = sem("diag_loaded")
        operand_ready = sem("operand_ready")
        zv_ready = sem("zv_ready")
        zg_ready = sem("zg_ready")
        zd_ready = sem("zd_ready")
        zv_used = sem("zv_used")
        zg_used = sem("zg_used")
        zd_used = sem("zd_used")
        h1_ready = sem("h1_ready")
        h2_ready = sem("h2_ready")
        h1_pooled = sem("h1_pooled")
        h2_pooled = sem("h2_pooled")
        h1_stored = sem("h1_stored")
        h_loaded = [sem(f"h_loaded{h}") for h in range(HALVES)]
        final_ready = sem("final_ready")
        out_ready = sem("out_ready")
        out_stored = sem("out_stored")

        X_DMAS, DIAG_DMAS, STORE_DMAS, H_DMAS, W_DMAS = 5, 4, 4, 3, 4

        def v_units(phase, b):
            return phase * DVE_B + (b + 1)

        def halves(phase, b, h):
            return phase * (DVE_B * HALVES) + (b * HALVES + h + 1)

        def steps(eng, step):
            step(0, 0, 1)
            with eng.Fori(0, PAIRS // 2 - 2) as j:
                step(j * 2 + 1, 1, j + 2)
                step(j * 2 + 2, 0, j + 2)
            for s in range(PAIRS - 3, PAIRS):
                step(s, s % 2, (s + 1) // 2 + 1)

        def g_unit(s, n, parity):
            n -= 1 if is_last(s) else 0
            return s * 3 + n, (parity + n) % G_RING

        def is_last(s):
            return isinstance(s, int) and s == PAIRS - 1

        def last_phase(s):
            return s * 3 + (2 if is_last(s) else 3)

        block = ctx.enter_context(nc.Block())

        @block.sync
        def _(sp):
            def rows(tensor, index, row, dims, run=BLK):
                whole = tensor[index]
                return bass.AP(tensor=whole.tensor, offset=whole.offset + row * T,
                               ap=[[step * T, n] for step, n in dims] + [[1, run * T]])

            def load_x(g, parity, part):
                loaded = (xa_loaded, xb_loaded)[part][parity]
                dst = xs[:, parity, :, part * BLK:(part + 1) * BLK, :]
                k_step = 2 * BLK if part == 0 else 0
                for h in range(HALVES):
                    sp.dma_start(dst[0:MAIN, h].rearrange("p a t -> p (a t)"),
                                 rows(x, g, h * XROWS + BLK + k_step,
                                      [[BLK, MATCH], [k_step, KS]])).then_inc(loaded, DMA)
                    two = BLK // 2
                    sp.dma_start(dst[SPARE:P, h].rearrange("p (v f) t -> p v (f t)", v=2),
                                 rows(x, g, h * XROWS + part * two,
                                      [[BLK, NSPARE], [NSPARE * BLK, 2]], two)
                                 ).then_inc(loaded, DMA)
                row, step = (0, 0) if part == 0 else (BLK, BLK)
                sp.dma_start(dst[MAIN:SPARE].rearrange("p h a t -> p h (a t)"),
                             rows(x, g, row, [[step, MATCH], [XROWS, HALVES]])
                             ).then_inc(loaded, DMA)

            def load_diag(g):
                xg = x[g]
                for dst, odd in ((diag0, 0), (diag1, 1)):
                    sp.dma_start(dst[0:FEAT], xg[:, 0:FEAT, :].rearrange("h r t -> r h t")
                                 ).then_inc(diag_loaded, DMA)
                    sp.dma_start(dst[FEAT:DIAG], xg[:, odd:FEAT:2, :].rearrange("h r t -> r h t")
                                 ).then_inc(diag_loaded, DMA)

            def spread_h1(g, parity):
                sp.wait_ge(h1_ready, g + 1)
                for h in range(HALVES):
                    sp.dma_start(h_dram[parity, h * HROWS:h * HROWS + FEAT, :], h1[h * FEAT:(h + 1) * FEAT, :]
                                 ).then_inc(h1_stored, DMA)
                    sp.dma_start(h_dram[parity, h * HROWS + FEAT:(h + 1) * HROWS, :],
                                 h1[h * FEAT + BLK:h * FEAT + BLK + KS * BLK, :]
                                 ).then_inc(h1_stored, DMA)

            def load_h(g, parity, stored):
                sp.wait_ge(h1_stored, stored)
                dst = hrep[:, :, :, :].rearrange("p h b t -> p h (b t)")
                for h in range(HALVES):
                    for lo, hi, row, dims in ((0, MAIN, 2 * BLK, [[BLK, MATCH], [BLK, KS]]),
                                              (MAIN, SPARE, BLK, [[BLK, MATCH]]),
                                              (SPARE, P, 0, [[0, NSPARE]])):
                        sp.dma_start(dst[lo:hi, h], rows(h_dram, parity, h * HROWS + row, dims)
                                     ).then_inc(h_loaded[h], DMA)

            sp.dma_start(w1s[:, :, :], w1).then_inc(w1_loaded, DMA)
            sp.dma_start(w1t_s, w1t).then_inc(w1_loaded, DMA)
            load_diag(0)
            load_x(0, 0, 1)
            load_x(0, 0, 0)
            sp.dma_start(w2s[:, :, :], w2).then_inc(weights_loaded, DMA)
            sp.dma_start(bias_s[:, :], bias).then_inc(weights_loaded, DMA)
            sp.dma_start(wfc_s[:, :, :], wfc).then_inc(weights_loaded, DMA)
            sp.dma_start(bfc_s[:, :], bfc).then_inc(weights_loaded, DMA)
            load_x(1, 1, 1)
            load_x(1, 1, 0)
            sp.wait_ge(zd_ready, 1)
            load_diag(1)
            spread_h1(0, 0)
            load_h(0, 0, STORE_DMAS * DMA)

            def value(v):
                if not isinstance(v, int):
                    sp.compute_val(v)
                return v

            def step(s, parity, nth):
                if is_last(s):
                    return
                phase_done = value(halves(s * 3 + 1, DVE_B - 1, 1))
                g_low_done = value(s * 6 + 6)
                phases_done = value(halves(s * 3 + 3, DVE_B - 1, 1))
                g_phases_done = value(s * 6 + 8)
                stored = value((s + 2) * (STORE_DMAS * DMA))
                more = not (isinstance(s, int) and s + 2 >= PAIRS)
                if more:
                    sp.wait_ge(zd_ready, s + 2)
                    load_diag(s + 2)
                    sp.wait_ge(zv_ready, phase_done)
                    sp.wait_ge(zg_ready, g_low_done)
                    load_x(s + 2, parity, 0)
                spread_h1(s + 1, 1 - parity)
                sp.wait_ge(operand_ready, phases_done)
                sp.wait_ge(zg_ready, g_phases_done)
                load_h(s + 1, 1 - parity, stored)
                if more:
                    sp.wait_ge(zv_ready, phases_done)
                    load_x(s + 2, parity, 1)

            steps(sp, step)
            sp.wait_ge(out_ready, 1)
            sp.dma_start(out, out_s[:, :].rearrange("h (g b) -> h g b", b=TILE_B)
                         ).then_inc(out_stored, DMA)
            sp.wait_ge(out_stored, DMA)

        @block.scalar
        def _(act):
            def fill(phase, source, h_loads=None):
                for b in range(DVE_B):
                    for h in range(HALVES):
                        if b == 0 and h_loads is not None:
                            act.wait_ge(h_loaded[h], h_loads)
                        if not (isinstance(phase, int) and phase == 0):
                            act.wait_ge(zv_ready, halves(phase - 1, b, h))
                        act.copy(operand[b][h][:, :], source(b, h)).then_inc(operand_ready, 1)

            def relu(layer, source, dest):
                return act.activation(dest[:, :], source[:, :], ACT.Relu,
                                      bias=bias_s[:, layer:layer + 1])

            def pool_rows(layer, g, h, done):
                if not (isinstance(g, int) and g == 0):
                    act.wait_ge(done, g)
                for b in range(TILE_B):
                    cols = slice(b * EMB, (b + 1) * EMB)
                    last = act.activation(unread[:, layer, cols], h[:, cols], ACT.Copy,
                                          accum_out=pooled[:, layer, g, b:b + 1])
                last.then_inc(done, 1)

            def layer1_end(g, phase):
                act.wait_ge(zv_used, v_units(phase, DVE_B - 1))
                if not (isinstance(g, int) and g == 0):
                    act.wait_ge(h1_stored, g * (STORE_DMAS * DMA))
                relu(0, acc1, h1).then_inc(h1_ready, 1)
                act.wait_ge(h1_ready, g + 1)
                pool_rows(0, g, h1, h1_pooled)

            def layer2_end(phase):
                act.wait_ge(zv_used, v_units(phase, DVE_B - 1))
                relu(1, acc2, h2).then_inc(h2_ready, 1)

            def layer2_pool(g):
                act.wait_ge(h2_ready, g + 1)
                pool_rows(1, g, h2, h2_pooled)

            act.wait_ge(xb_loaded[0], X_DMAS * DMA)
            fill(0, lambda b, h: xs[:, 0, h, BLK + b, :])
            act.wait_ge(weights_loaded, W_DMAS * DMA)
            layer1_end(0, 0)

            def step(s, parity, nth):
                fill(s * 3 + 1, lambda b, h: hrep[:, h, b, :], (s + 1) * (H_DMAS * DMA))
                first = isinstance(s, int) and s == 0
                if not first:
                    layer2_end(s * 3)
                if not is_last(s):
                    act.wait_ge(xb_loaded[1 - parity], nth * (X_DMAS * DMA))
                    fill(s * 3 + 2, lambda b, h: xs[:, 1 - parity, h, BLK + b, :])
                if not first:
                    layer2_pool(s - 1)
                fill(last_phase(s), lambda b, h: hrep[:, h, b, :])
                if not is_last(s):
                    layer1_end(s + 1, s * 3 + 2)

            steps(act, step)
            layer2_end(last_phase(PAIRS - 1))
            layer2_pool(PAIRS - 1)
            act.wait_ge(final_ready, 1)
            act.activation(out_s[:, :], acc1[0:HALVES, 0:PAIRS * TILE_B], ACT.Identity,
                           bias=bfc_s[:, :]).then_inc(out_ready, 1)

        @block.vector
        def _(dve):
            def products(phase, parity, part):
                for b in range(DVE_B):
                    if not (isinstance(phase, int) and phase == 0):
                        dve.wait_ge(zv_used, v_units(phase - 1, b))
                    for h in range(HALVES):
                        dve.wait_ge(operand_ready, halves(phase, b, h))
                        dve.tensor_tensor(
                            zv[:, b, h, :, :], xs[:, parity, h, part * BLK:(part + 1) * BLK, :],
                            operand[b][h][:, :].unsqueeze(1).broadcast_to((P, BLK, T)),
                            ALU.mult).then_inc(zv_ready, 1)

            dve.wait_ge(w1_loaded, 2 * DMA)
            dve.tensor_tensor(w1s[:, :, :], w1s[:, :, :], w1t_s, ALU.add).then_inc(w1_summed, 1)
            dve.wait_ge(xa_loaded[0], X_DMAS * DMA)
            products(0, 0, 0)

            def step(s, parity, nth):
                products(s * 3 + 1, parity, 0)
                if not is_last(s):
                    dve.wait_ge(xa_loaded[1 - parity], nth * (X_DMAS * DMA))
                    products(s * 3 + 2, 1 - parity, 0)
                products(last_phase(s), parity, 1)

            steps(dve, step)

        @block.gpsimd
        def _(pool):
            def products(number, buffer, parity, part, value):
                if not (isinstance(number, int) and number < G_RING):
                    pool.wait_ge(zg_used, number - (G_RING - 1))
                for h in range(HALVES):
                    pool.tensor_tensor(
                        zg[:, buffer, h, :, :], xs[:, parity, h, part * BLK:(part + 1) * BLK, :],
                        value(h).unsqueeze(1).broadcast_to((P, BLK, T)), ALU.mult
                    ).then_inc(zg_ready, 1)

            def diagonal(g):
                pool.wait_ge(diag_loaded, (g + 1) * (DIAG_DMAS * DMA))
                if not (isinstance(g, int) and g == 0):
                    pool.wait_ge(zd_used, g)
                pool.tensor_tensor(zd[:, :, :], diag0[:, :, :], diag1[:, :, :], ALU.mult
                                   ).then_inc(zd_ready, 1)

            pool.wait_ge(xa_loaded[0], X_DMAS * DMA)
            pool.wait_ge(xb_loaded[0], X_DMAS * DMA)
            diagonal(0)
            pool.wait_ge(w1_summed, 1)
            products(0, 0, 0, 0, lambda h: xs[:, 0, h, SLOTS - 1, :])
            diagonal(1)

            def step(s, parity, nth):
                if not is_last(s):
                    pool.wait_ge(xa_loaded[1 - parity], nth * (X_DMAS * DMA))
                    pool.wait_ge(xb_loaded[1 - parity], nth * (X_DMAS * DMA))
                    products(*g_unit(s, 1, parity), 1 - parity, 0,
                             lambda h: xs[:, 1 - parity, h, SLOTS - 1, :])
                for h in range(HALVES):
                    pool.wait_ge(h_loaded[h], (s + 1) * (H_DMAS * DMA))
                for part in range(2):
                    products(*g_unit(s, 2 + part, parity), parity, part,
                             lambda h: hrep[:, h, BLK - 1, :])
                if not (isinstance(s, int) and s + 2 >= PAIRS):
                    diagonal(s + 2)

            steps(pool, step)

        @block.tensor
        def _(pe):
            def chunk(acc, weights, z, first, last):
                rows = z(0).shape[0]
                for h in range(HALVES):
                    mm = pe.matmul(acc[h * FEAT:(h + 1) * FEAT, :], weights[0:rows], z(h),
                                   start=first, stop=last)
                return mm

            def unit(acc, weights, z, first, last):
                for a in range(BLK):
                    mm = chunk(acc, weights[:, a], lambda h: z[:, h, a, :],
                               first and a == 0, last and a == BLK - 1)
                return mm

            def from_vector(phase, b, acc, weights, first=False, last=False):
                pe.wait_ge(zv_ready, halves(phase, b, 1))
                unit(acc, weights[:, b * BLK:(b + 1) * BLK], zv[:, b], first, last
                     ).then_inc(zv_used, 1)

            def from_gpsimd(number, buffer, acc, weights):
                pe.wait_ge(zg_ready, number * HALVES + HALVES)
                unit(acc, weights[:, (BLK - 1) * BLK:BLK * BLK], zg[:, buffer], False, False
                     ).then_inc(zg_used, 1)

            def layer1(phase, number, buffer):
                from_vector(phase, 0, acc1, w1s)
                from_vector(phase, 1, acc1, w1s)
                from_gpsimd(number, buffer, acc1, w1s)
                from_vector(phase, 2, acc1, w1s, last=True)

            def diagonal(g):
                pe.wait_ge(zd_ready, g + 1)
                if not (isinstance(g, int) and g == 0):
                    pe.wait_ge(h1_ready, g)
                chunk(acc1, w1s[0:DIAG, C1], lambda h: zd[:, h, :], True, False
                      ).then_inc(zd_used, 1)

            pe.wait_ge(w1_summed, 1)
            diagonal(0)
            layer1(0, 0, 0)
            pe.wait_ge(weights_loaded, W_DMAS * DMA)

            def step(s, parity, nth):
                if not is_last(s):
                    diagonal(s + 1)
                if not (isinstance(s, int) and s == 0):
                    pe.wait_ge(h2_ready, s)
                low, high = w2s[:, 0:C1], w2s[:, C1:C2]
                for b in range(DVE_B):
                    from_vector(s * 3 + 1, b, acc2, low, first=b == 0)
                if not is_last(s):
                    layer1(s * 3 + 2, *g_unit(s, 1, parity))
                from_vector(last_phase(s), 0, acc2, high)
                from_gpsimd(*g_unit(s, 2, parity), acc2, low)
                from_vector(last_phase(s), 1, acc2, high)
                from_gpsimd(*g_unit(s, 3, parity), acc2, high)
                from_vector(last_phase(s), 2, acc2, high, last=True)

            steps(pe, step)
            pe.wait_ge(h1_pooled, PAIRS)
            pe.wait_ge(h2_pooled, PAIRS)
            for layer in range(2):
                mm = pe.matmul(acc1[0:HALVES, 0:PAIRS * TILE_B], wfc_s[:, layer, :],
                               pooled[:, layer, :, :].rearrange("p g b -> p (g b)"),
                               start=(layer == 0), stop=(layer == 1))
            mm.then_inc(final_ready, 1)


def lay_out(r_x, W1, b1, W2, b2, Wfc, bfc):
    feats, hblk = partition_features()
    order = feature_order()
    tiles = r_x.reshape(PAIRS, HALVES, TILE_B, FEAT, EMB).transpose(0, 1, 3, 2, 4)
    tiles = tiles.reshape(PAIRS, HALVES, NBLK, BLK, T)
    x = tiles[:, :, ORDER].reshape(PAIRS, HALVES, XROWS, T)

    W1 = W1.reshape(FEAT, FEAT, FEAT)[order]
    W2 = W2.reshape(FEAT, FEAT, FEAT)[order]
    w1 = np.zeros((P, C1 + 1, FEAT), W1.dtype)
    w1t = np.zeros_like(w1)
    for b in range(BLK):
        for a in range(BLK):
            i, j = feats[:, a], feats[:, BLK + b]
            use = (np.arange(P) < SPARE) | (i // BLK == j // BLK)
            c = b * BLK + a
            w1[use, c] = W1[:, i, j].T[use]
            w1t[use, c] = W1[:, j, i].T[use]
    i = np.concatenate([order, order[0::2]])
    j = np.concatenate([order, order[1::2]])
    w1[:DIAG, C1] = W1[:, i, j].T
    w1t[FEAT:DIAG, C1] = W1[:, j, i].T[FEAT:]
    w2 = np.zeros((P, C2, FEAT), W2.dtype)
    for s in range(SLOTS):
        for b in range(BLK):
            c = (s // BLK) * C1 + b * BLK + s % BLK
            w2[:, c] = W2[:, feats[:, s], hblk * BLK + b].T
    bias = np.tile(np.stack([b1[order], b2[order]], axis=1), (HALVES, 1))
    wfc = np.zeros((P, 2, HALVES), Wfc.dtype)
    for h in range(HALVES):
        wfc[h * FEAT:(h + 1) * FEAT, :, h] = Wfc[0].reshape(2, FEAT)[:, order].T
    return {"x": x, "w1": w1, "w1t": w1t, "w2": w2, "bias": bias, "wfc": wfc,
            "bfc": np.tile(bfc.reshape(1, 1), (HALVES, 1))}


def kernel(r_x, L0_rec_W1, L0_rec_b1, L0_rec_W2, L0_rec_b2, L0_rec_Wfc, L0_rec_bfc):
    import concourse.bacc as bacc
    from concourse.bass_utils import run_bass_kernel_spmd

    given = (r_x, L0_rec_W1, L0_rec_b1, L0_rec_W2, L0_rec_b2, L0_rec_Wfc, L0_rec_bfc)
    arrays = {n: np.ascontiguousarray(a) for n, a in lay_out(*map(np.asarray, given)).items()}
    nc = bacc.Bacc("TRN2", target_bir_lowering=False, num_devices=1)
    args = [nc.dram_tensor(n, a.shape, F32, kind="ExternalInput").ap() for n, a in arrays.items()]
    out = nc.dram_tensor("out", (BATCH, 1), F32, kind="ExternalOutput").ap()
    build(nc, *args, out.rearrange("(g h b) o -> h g (b o)", h=HALVES, b=TILE_B))
    result = run_bass_kernel_spmd(nc, [arrays], core_ids=[0])
    return result.results[0]["out"]
```

```python
from contextlib import ExitStack

import numpy as np
import concourse.bass as bass
from concourse import mybir

ALU = mybir.AluOpType
ACT = mybir.ActivationFunctionType
F32 = mybir.dt.float32

P = 128
FEAT = 64
EMB = 64
BATCH = 512
TILE_B = 8
T = TILE_B * EMB
HALVES = 2
PAIRS = BATCH // (TILE_B * HALVES)
BLK = 4
NBLK = FEAT // BLK
MATCH = NBLK - 1
MAIN = MATCH * (NBLK // 2 - 1)
SPARE = MATCH * (NBLK // 2)
NSPARE = P - SPARE
SLOTS = 2 * BLK
DIAG = FEAT + FEAT // 2
C1 = BLK * BLK
C2 = SLOTS * BLK

KS = NBLK // 2 - 1
ORDER = [MATCH] + 2 * list(range(MATCH))
ORDER = ORDER[:1 + MATCH + 2 * KS]
XROWS = len(ORDER) * BLK
HROWS = (1 + MATCH + KS) * BLK

OPERANDS = 3
V_RING = 4
G_RING = 2
V_STEP, G_STEP = 8, 4
DMA = 16


def partition_features():
    feats = np.zeros((P, SLOTS), np.int64)
    hblk = np.zeros(P, np.int64)
    four = np.arange(BLK)
    for n in range(MATCH):
        for k in range(1, KS + 1):
            p = n * KS + k - 1
            feats[p] = np.concatenate([(n + 2 * k) % MATCH * BLK + four, n * BLK + four])
            hblk[p] = (n + k) % MATCH
        feats[MAIN + n] = np.concatenate([MATCH * BLK + four, n * BLK + four])
        hblk[MAIN + n] = n
    for s in range(NSPARE):
        one, two = ORDER[s] * BLK, ORDER[s + NSPARE] * BLK
        feats[SPARE + s] = [one, one + 1, two, two + 1, one + 2, one + 3, two + 2, two + 3]
        hblk[SPARE + s] = MATCH
    return feats, hblk


def feature_order():
    return np.array([ORDER[r // BLK] * BLK + r % BLK for r in range(FEAT)])


def build(nc, x, w1, w1t, w2, bias, wfc, bfc, out):
    with ExitStack() as ctx:
        def sb(name, shape):
            return ctx.enter_context(nc.sbuf_tensor(name, shape, F32))

        def sem(name):
            return ctx.enter_context(nc.semaphore(name))

        xs = sb("xs", [P, 2, HALVES, SLOTS, T])
        hrep = sb("hrep", [P, HALVES, BLK, T])
        diag0 = sb("diag0", [DIAG, HALVES, T])
        diag1 = sb("diag1", [DIAG, HALVES, T])
        zv = sb("zv", [P, V_RING, HALVES, BLK, T])
        zg = sb("zg", [P, G_RING, HALVES, BLK, T])
        zd = sb("zd", [DIAG, HALVES, T])
        w1s = sb("w1s", [P, C1 + 1, FEAT])
        w2s = sb("w2s", [P, C2, FEAT])
        bias_s = sb("bias_s", [P, 2])
        wfc_s = sb("wfc_s", [P, 2, HALVES])
        bfc_s = sb("bfc_s", [HALVES, 1])
        h1 = sb("h1", [P, T])
        h2 = sb("h2", [P, T])
        pooled = sb("pooled", [P, 2, PAIRS, TILE_B])
        out_s = sb("out_s", [HALVES, PAIRS * TILE_B])
        w1t_s = zg[:, 0, 0].rearrange("p b t -> p (b t)")[:, 0:(C1 + 1) * FEAT].rearrange(
            "p (c o) -> p c o", o=FEAT)

        operand = [[ctx.enter_context(nc.psum_tensor(f"operand{b}{h}", [P, T], F32))
                    for h in range(HALVES)] for b in range(OPERANDS)]
        acc1 = ctx.enter_context(nc.psum_tensor("acc1", [P, T], F32))
        acc2 = ctx.enter_context(nc.psum_tensor("acc2", [P, T], F32))

        h_dram = nc.dram_tensor("h_scratch", [2, HALVES * HROWS, T], F32, kind="Internal").ap()

        weights_loaded = sem("weights_loaded")
        w1_loaded = sem("w1_loaded")
        w1_summed = sem("w1_summed")
        w2_loaded = sem("w2_loaded")
        x_first = [[sem(f"x_first{g}{h}") for h in range(HALVES)] for g in range(2)]
        x_rest = [sem(f"x_rest{g}") for g in range(2)]
        xa_loaded = [sem(f"xa_loaded{i}") for i in range(2)]
        xb_loaded = [sem(f"xb_loaded{i}") for i in range(2)]
        diag_loaded = sem("diag_loaded")
        operand_ready = sem("operand_ready")
        zv_ready = sem("zv_ready")
        zg_ready = sem("zg_ready")
        zd_ready = sem("zd_ready")
        zv_used = sem("zv_used")
        zg_used = sem("zg_used")
        zd_used = sem("zd_used")
        h1_ready = sem("h1_ready")
        h2_ready = sem("h2_ready")
        h1_pooled = sem("h1_pooled")
        h2_pooled = sem("h2_pooled")
        h1_stored = sem("h1_stored")
        h_loaded = [sem(f"h_loaded{h}") for h in range(HALVES)]
        h3_loaded = sem("h3_loaded")
        final_ready = sem("final_ready")
        out_ready = sem("out_ready")
        out_stored = sem("out_stored")

        X_DMAS, DIAG_DMAS, STORE_DMAS, H_DMAS, H3_DMAS, W_DMAS = 5, 4, 4, 3, 4, 3
        FIRST_DMAS, REST_DMAS = 5, 2

        LOW, ONE, HIGH = "low", "one", "high"
        V_VALUES = {LOW: 2, ONE: 3, HIGH: 3}

        def is_last(s):
            return isinstance(s, int) and s == PAIRS - 1

        def order(s):
            if isinstance(s, int) and s <= 0:
                return (ONE,) if s < 0 else (ONE, LOW, HIGH)
            return (LOW, HIGH) if is_last(s) else (LOW, ONE, HIGH)

        def in_step(s, kind, b):
            before = order(s)[:order(s).index(kind)]
            return sum(V_VALUES[k] for k in before) + b

        def v_unit(s, kind, b):
            if isinstance(s, int) and s < 0:
                return b
            return s * V_STEP + (V_VALUES[ONE] + in_step(s, kind, b))

        def v_buffer(s, kind, b):
            assert V_STEP % V_RING == 0 and G_STEP % G_RING == 0
            if isinstance(s, int) and s < 0:
                return b
            return (V_VALUES[ONE] + in_step(s, kind, b)) % V_RING

        def v_before(s, kind, b):
            for k in reversed(order(s)[:order(s).index(kind)]):
                if b < V_VALUES[k]:
                    return v_unit(s, k, b)
            if isinstance(s, int) and s <= 0:
                return None if s < 0 else v_unit(-1, ONE, b)
            return v_unit(s - 1, HIGH, b)

        def g_order(s):
            if isinstance(s, int) and s <= 0:
                return ((ONE, 3),) if s < 0 else ((ONE, 3), (LOW, 2), (LOW, 3), (HIGH, 3))
            one = () if is_last(s) else ((ONE, 3),)
            return ((LOW, 2),) + one + ((LOW, 3), (HIGH, 3))

        def g_unit(s, kind, b):
            if isinstance(s, int) and s < 0:
                return 0, 0
            n = 1 + g_order(s).index((kind, b))
            return s * G_STEP + n, n % G_RING

        V, G = "vector", "gpsimd"

        def pe_order(s):
            if isinstance(s, int) and s < 0:
                return ((V, ONE, 0), (V, ONE, 1), (V, ONE, 2), (G, ONE, 3))
            if isinstance(s, int) and s == 0:
                return ((V, ONE, 0), (V, ONE, 1), (V, ONE, 2), (G, ONE, 3), (V, LOW, 0),
                        (V, LOW, 1), (G, LOW, 2), (V, HIGH, 0), (G, LOW, 3), (V, HIGH, 1),
                        (G, HIGH, 3), (V, HIGH, 2))
            turns = ((V, LOW, 0), (V, LOW, 1), (G, LOW, 2), (V, ONE, 0), (V, ONE, 1), (V, ONE, 2),
                     (G, ONE, 3), (V, HIGH, 0), (G, LOW, 3), (V, HIGH, 1), (G, HIGH, 3),
                     (V, HIGH, 2))
            return tuple(t for t in turns if t[1] != ONE) if is_last(s) else turns

        def made(unit, h=HALVES - 1):
            return unit * HALVES + (h + 1)

        def steps(eng, step):
            step(0, 0, None)
            with eng.Fori(0, PAIRS // 2 - 2) as j:
                step(j * 2 + 1, 1, j + 1)
                step(j * 2 + 2, 0, j + 1)
            for s in range(PAIRS - 3, PAIRS):
                step(s, s % 2, (s + 1) // 2)

        block = ctx.enter_context(nc.Block())

        @block.sync
        def _(sp):
            def rows(tensor, index, row, dims, run=BLK):
                whole = tensor[index]
                return bass.AP(tensor=whole.tensor, offset=whole.offset + row * T,
                               ap=[[step * T, n] for step, n in dims] + [[1, run * T]])

            def load_x(g, parity, part):
                loaded = (xa_loaded, xb_loaded)[part][parity]
                dst = xs[:, parity, :, part * BLK:(part + 1) * BLK, :]
                k_step = 2 * BLK if part == 0 else 0
                for h in range(HALVES):
                    sp.dma_start(dst[0:MAIN, h].rearrange("p a t -> p (a t)"),
                                 rows(x, g, h * XROWS + BLK + k_step,
                                      [[BLK, MATCH], [k_step, KS]])).then_inc(loaded, DMA)
                    two = BLK // 2
                    sp.dma_start(dst[SPARE:P, h].rearrange("p (v f) t -> p v (f t)", v=2),
                                 rows(x, g, h * XROWS + part * two,
                                      [[BLK, NSPARE], [NSPARE * BLK, 2]], two)
                                 ).then_inc(loaded, DMA)
                row, step = (0, 0) if part == 0 else (BLK, BLK)
                sp.dma_start(dst[MAIN:SPARE].rearrange("p h a t -> p h (a t)"),
                             rows(x, g, row, [[step, MATCH], [XROWS, HALVES]])
                             ).then_inc(loaded, DMA)

            def load_x_start(g):
                lo = BLK + 1
                for h in range(HALVES):
                    loaded = x_first[g][h]
                    dst = xs[:, g, h].rearrange("p f t -> p (f t)")
                    row = h * XROWS
                    sp.dma_start(dst[0:MAIN, 0:BLK * T],
                                 rows(x, g, row + 3 * BLK, [[BLK, MATCH], [2 * BLK, KS]])
                                 ).then_inc(loaded, DMA)
                    sp.dma_start(dst[0:MAIN, BLK * T:lo * T],
                                 rows(x, g, row + BLK, [[BLK, MATCH], [0, KS]], 1)
                                 ).then_inc(loaded, DMA)
                    sp.dma_start(dst[MAIN:SPARE, 0:BLK * T], rows(x, g, row, [[0, MATCH]])
                                 ).then_inc(loaded, DMA)
                    sp.dma_start(dst[MAIN:SPARE, BLK * T:], rows(x, g, row + BLK, [[BLK, MATCH]])
                                 ).then_inc(loaded, DMA)
                    two = BLK // 2
                    sp.dma_start(
                        xs[SPARE:P, g, h].rearrange("p (u v f) t -> p u v (f t)", u=2, v=2),
                        rows(x, g, row, [[BLK, NSPARE], [two, 2], [NSPARE * BLK, 2]], two)
                    ).then_inc(loaded, DMA)
                for h in range(HALVES):
                    sp.dma_start(xs[0:MAIN, g, h, lo:, :].rearrange("p f t -> p (f t)"),
                                 rows(x, g, h * XROWS + lo, [[BLK, MATCH], [0, KS]], BLK - 1)
                                 ).then_inc(x_rest[g], DMA)

            def load_diag(g):
                xg = x[g]
                for dst, odd in ((diag0, 0), (diag1, 1)):
                    sp.dma_start(dst[0:FEAT], xg[:, 0:FEAT, :].rearrange("h r t -> r h t")
                                 ).then_inc(diag_loaded, DMA)
                    sp.dma_start(dst[FEAT:DIAG], xg[:, odd:FEAT:2, :].rearrange("h r t -> r h t")
                                 ).then_inc(diag_loaded, DMA)

            def spread_h1(g, parity):
                sp.wait_ge(h1_ready, g + 1)
                for h in range(HALVES):
                    sp.dma_start(h_dram[parity, h * HROWS:h * HROWS + FEAT, :],
                                 h1[h * FEAT:(h + 1) * FEAT, :]
                                 ).then_inc(h1_stored, DMA)
                    sp.dma_start(h_dram[parity, h * HROWS + FEAT:(h + 1) * HROWS, :],
                                 h1[h * FEAT + BLK:h * FEAT + BLK + KS * BLK, :]
                                 ).then_inc(h1_stored, DMA)

            def load_h(parity):
                first = BLK - 1
                for h in range(HALVES):
                    for lo, hi, row, dims in ((0, MAIN, 2 * BLK, [[BLK, MATCH], [BLK, KS]]),
                                              (MAIN, SPARE, BLK, [[BLK, MATCH]]),
                                              (SPARE, P, 0, [[0, NSPARE]])):
                        sp.dma_start(hrep[lo:hi, h, 0:first, :].rearrange("p b t -> p (b t)"),
                                     rows(h_dram, parity, h * HROWS + row, dims, first)
                                     ).then_inc(h_loaded[h], DMA)

            def load_h3(parity):
                b = BLK - 1
                for h in range(HALVES):
                    sp.dma_start(hrep[0:MAIN, h, b, :],
                                 rows(h_dram, parity, h * HROWS + 2 * BLK + b,
                                      [[BLK, MATCH], [BLK, KS]], 1)).then_inc(h3_loaded, DMA)
                sp.dma_start(hrep[MAIN:SPARE, :, b, :],
                             rows(h_dram, parity, BLK + b, [[BLK, MATCH], [HROWS, HALVES]], 1)
                             ).then_inc(h3_loaded, DMA)
                sp.dma_start(hrep[SPARE:P, :, b, :],
                             rows(h_dram, parity, b, [[0, NSPARE], [HROWS, HALVES]], 1)
                             ).then_inc(h3_loaded, DMA)

            sp.dma_start(w1s[:, :, :], w1).then_inc(w1_loaded, DMA)
            sp.dma_start(w1t_s, w1t).then_inc(w1_loaded, DMA)
            load_diag(0)
            load_x_start(0)
            sp.dma_start(bias_s[:, :], bias).then_inc(weights_loaded, DMA)
            sp.dma_start(wfc_s[:, :, :], wfc).then_inc(weights_loaded, DMA)
            sp.dma_start(bfc_s[:, :], bfc).then_inc(weights_loaded, DMA)
            sp.wait_ge(zd_ready, 1)
            load_diag(1)
            load_x_start(1)
            sp.dma_start(w2s[:, :, :], w2).then_inc(w2_loaded, DMA)
            spread_h1(0, 0)
            sp.wait_ge(h1_stored, STORE_DMAS * DMA)
            load_h(0)
            load_h3(0)

            def value(v):
                if not isinstance(v, int):
                    sp.compute_val(v)
                return v

            def step(s, parity, nth):
                if is_last(s):
                    return
                more = not (isinstance(s, int) and s + 2 >= PAIRS)
                v_low_made = value(made(v_unit(s, LOW, 1)))
                v_high_filled = value(made(v_unit(s, HIGH, 2)))
                g_low2_made, g_low3_made, g_high_made = (
                    value(made(g_unit(s, kind, b)[0]))
                    for kind, b in ((LOW, 2), (LOW, 3), (HIGH, 3)))
                stored = value((s + 2) * (STORE_DMAS * DMA))
                if more:
                    sp.wait_ge(zd_ready, s + 2)
                    load_diag(s + 2)
                for kind in order(s):
                    if kind == LOW and more:
                        sp.wait_ge(zv_ready, v_low_made)
                        sp.wait_ge(zg_ready, g_low3_made)
                        load_x(s + 2, parity, 0)
                    if kind == ONE:
                        spread_h1(s + 1, 1 - parity)
                sp.wait_ge(h1_stored, stored)
                sp.wait_ge(operand_ready, v_high_filled)
                sp.wait_ge(zg_ready, g_low2_made)
                load_h(1 - parity)
                sp.wait_ge(zg_ready, g_high_made)
                load_h3(1 - parity)
                if more:
                    sp.wait_ge(zv_ready, v_high_filled)
                    load_x(s + 2, parity, 1)

            steps(sp, step)
            sp.wait_ge(out_ready, 1)
            sp.dma_start(out, out_s[:, :].rearrange("h (g b) -> h g b", b=TILE_B)
                         ).then_inc(out_stored, DMA)
            sp.wait_ge(out_stored, DMA)

        @block.scalar
        def _(act):
            def fill(s, kind, source, start=None, h_loads=None):
                for b in range(V_VALUES[kind]):
                    if b == 1 and start is not None:
                        act.wait_ge(x_rest[start], REST_DMAS * DMA)
                    for h in range(HALVES):
                        if b == 0 and start is not None:
                            act.wait_ge(x_first[start][h], FIRST_DMAS * DMA)
                        if b == 0 and h_loads is not None:
                            act.wait_ge(h_loaded[h], h_loads)
                        if v_before(s, kind, b) is not None:
                            act.wait_ge(zv_ready, made(v_before(s, kind, b), h))
                        act.copy(operand[b][h][:, :], source(b, h)).then_inc(operand_ready, 1)

            def relu(layer, source, dest):
                return act.activation(dest[:, :], source[:, :], ACT.Relu,
                                      bias=bias_s[:, layer:layer + 1])

            def pool_rows(layer, g, h, done):
                for b in range(TILE_B):
                    cols = slice(b * EMB, (b + 1) * EMB)
                    last = act.activation(h2[:, cols], h[:, cols], ACT.Copy,
                                          accum_out=pooled[:, layer, g, b:b + 1])
                last.then_inc(done, 1)

            def layer1_end(s):
                act.wait_ge(zg_used, g_unit(s, ONE, 3)[0] + 1)
                if not (isinstance(s, int) and s < 0):
                    act.wait_ge(h1_stored, (s + 1) * (STORE_DMAS * DMA))
                relu(0, acc1, h1).then_inc(h1_ready, 1)
                act.wait_ge(h1_ready, s + 2)
                if not (isinstance(s, int) and s < 1):
                    act.wait_ge(h2_pooled, s)
                if not (isinstance(s, int) and s < 0):
                    act.wait_ge(h1_pooled, s + 1)
                pool_rows(0, s + 1, h1, h1_pooled)

            def layer2_end(s):
                act.wait_ge(zv_used, v_unit(s, HIGH, 2) + 1)
                act.wait_ge(h1_pooled, s + (1 if is_last(s) else 2))
                relu(1, acc2, h2).then_inc(h2_ready, 1)

            def layer2_pool(s):
                act.wait_ge(h2_ready, s + 1)
                pool_rows(1, s, h2, h2_pooled)

            fill(-1, ONE, lambda b, h: xs[:, 0, h, BLK + b, :], start=0)
            act.wait_ge(weights_loaded, W_DMAS * DMA)

            def step(s, parity, nth):
                first = isinstance(s, int) and s == 0
                for kind in order(s):
                    if kind == LOW:
                        fill(s, LOW, lambda b, h: hrep[:, h, b, :],
                             h_loads=(s + 1) * (H_DMAS * DMA))
                        if not first:
                            layer2_end(s - 1)
                    if kind == ONE:
                        if not first:
                            act.wait_ge(xb_loaded[1 - parity], nth * (X_DMAS * DMA))
                        fill(s, ONE, lambda b, h: xs[:, 1 - parity, h, BLK + b, :],
                             start=1 if first else None)
                        if first:
                            layer1_end(-1)
                    if kind == HIGH:
                        if not first:
                            layer2_pool(s - 1)
                        fill(s, HIGH, lambda b, h: hrep[:, h, b, :])
                if not is_last(s):
                    layer1_end(s)

            steps(act, step)
            layer2_end(PAIRS - 1)
            act.wait_ge(final_ready, 1)
            act.activation(out_s[:, :], acc1[0:HALVES, 0:PAIRS * TILE_B], ACT.Identity,
                           bias=bfc_s[:, :]).then_inc(out_ready, 1)

        @block.vector
        def _(dve):
            def products(s, kind, parity, start=None):
                lo = BLK if kind == HIGH else 0
                for b in range(V_VALUES[kind]):
                    unit, buffer = v_unit(s, kind, b), v_buffer(s, kind, b)
                    if not (isinstance(unit, int) and unit < V_RING):
                        dve.wait_ge(zv_used, unit - (V_RING - 1))
                    for h in range(HALVES):
                        if b == 0 and start is not None:
                            dve.wait_ge(x_first[start][h], FIRST_DMAS * DMA)
                        dve.wait_ge(operand_ready, made(unit, h))
                        dve.tensor_tensor(
                            zv[:, buffer, h, :, :], xs[:, parity, h, lo:lo + BLK, :],
                            operand[b][h][:, :].unsqueeze(1).broadcast_to((P, BLK, T)),
                            ALU.mult).then_inc(zv_ready, 1)

            dve.wait_ge(w1_loaded, 2 * DMA)
            dve.tensor_tensor(w1s[:, :, :], w1s[:, :, :], w1t_s, ALU.add).then_inc(w1_summed, 1)
            products(-1, ONE, 0, start=0)

            def step(s, parity, nth):
                first = isinstance(s, int) and s == 0
                for kind in order(s):
                    if kind == ONE and not first:
                        dve.wait_ge(xa_loaded[1 - parity], nth * (X_DMAS * DMA))
                    products(s, kind, 1 - parity if kind == ONE else parity,
                             start=1 if kind == ONE and first else None)

            steps(dve, step)
            dve.wait_ge(h2_ready, PAIRS)
            dve.tensor_reduce(pooled[:, 1, PAIRS - 1, :],
                              h2[:, :].rearrange("p (b d) -> p b d", d=EMB),
                              mybir.AxisListType.X, ALU.add).then_inc(h2_pooled, 1)

        @block.gpsimd
        def _(pool):
            def products(s, kind, b, parity, value):
                number, buffer = g_unit(s, kind, b)
                lo = BLK if kind == HIGH else 0
                if not (isinstance(number, int) and number < G_RING):
                    pool.wait_ge(zg_used, number - (G_RING - 1))
                for h in range(HALVES):
                    pool.tensor_tensor(
                        zg[:, buffer, h, :, :], xs[:, parity, h, lo:lo + BLK, :],
                        value(h).unsqueeze(1).broadcast_to((P, BLK, T)), ALU.mult
                    ).then_inc(zg_ready, 1)

            def diagonal(g):
                pool.wait_ge(diag_loaded, (g + 1) * (DIAG_DMAS * DMA))
                if not (isinstance(g, int) and g == 0):
                    pool.wait_ge(zd_used, g)
                pool.tensor_tensor(zd[:, :, :], diag0[:, :, :], diag1[:, :, :], ALU.mult
                                   ).then_inc(zd_ready, 1)

            def start_loaded(g):
                for h in range(HALVES):
                    pool.wait_ge(x_first[g][h], FIRST_DMAS * DMA)
                pool.wait_ge(x_rest[g], REST_DMAS * DMA)

            def from_x(parity):
                return lambda h: xs[:, parity, h, SLOTS - 1, :]

            def from_h(b):
                return lambda h: hrep[:, h, b, :]

            diagonal(0)
            pool.wait_ge(w1_summed, 1)
            start_loaded(0)
            products(-1, ONE, 3, 0, from_x(0))
            diagonal(1)

            def step(s, parity, nth):
                for kind, b in g_order(s):
                    if kind == ONE:
                        if isinstance(s, int) and s == 0:
                            start_loaded(1)
                        else:
                            pool.wait_ge(xa_loaded[1 - parity], nth * (X_DMAS * DMA))
                            pool.wait_ge(xb_loaded[1 - parity], nth * (X_DMAS * DMA))
                        products(s, kind, b, 1 - parity, from_x(1 - parity))
                        continue
                    if (kind, b) == (LOW, 2):
                        for h in range(HALVES):
                            pool.wait_ge(h_loaded[h], (s + 1) * (H_DMAS * DMA))
                    if (kind, b) == (LOW, 3):
                        pool.wait_ge(h3_loaded, (s + 1) * (H3_DMAS * DMA))
                    products(s, kind, b, parity, from_h(b))
                if not (isinstance(s, int) and s + 2 >= PAIRS):
                    diagonal(s + 2)

            steps(pool, step)

        @block.tensor
        def _(pe):
            def chunk(acc, weights, z, first, last):
                rows = z(0).shape[0]
                for h in range(HALVES):
                    mm = pe.matmul(acc[h * FEAT:(h + 1) * FEAT, :], weights[0:rows], z(h),
                                   start=first, stop=last)
                return mm

            def unit(acc, weights, z, first, last):
                for a in range(BLK):
                    mm = chunk(acc, weights[:, a], lambda h: z[:, h, a, :],
                               first and a == 0, last and a == BLK - 1)
                return mm

            def sum_units(s):
                for engine, kind, b in pe_order(s):
                    acc, chunks = {ONE: (acc1, w1s[:, 0:C1]), LOW: (acc2, w2s[:, 0:C1]),
                                   HIGH: (acc2, w2s[:, C1:C2])}[kind]
                    first = (kind, b) == (LOW, 0)
                    last = (kind, b) in ((ONE, 3), (HIGH, 2))
                    w = chunks[:, b * BLK:(b + 1) * BLK]
                    if first and not (isinstance(s, int) and s == 0):
                        pe.wait_ge(h2_ready, s)
                    if engine == V:
                        pe.wait_ge(zv_ready, made(v_unit(s, kind, b)))
                        unit(acc, w, zv[:, v_buffer(s, kind, b)], first, last
                             ).then_inc(zv_used, 1)
                    else:
                        number, buffer = g_unit(s, kind, b)
                        pe.wait_ge(zg_ready, made(number))
                        unit(acc, w, zg[:, buffer], first, last).then_inc(zg_used, 1)

            def diagonal(g):
                pe.wait_ge(zd_ready, g + 1)
                if not (isinstance(g, int) and g == 0):
                    pe.wait_ge(h1_ready, g)
                chunk(acc1, w1s[0:DIAG, C1], lambda h: zd[:, h, :], True, False
                      ).then_inc(zd_used, 1)

            pe.wait_ge(w1_summed, 1)
            diagonal(0)
            sum_units(-1)
            pe.wait_ge(w2_loaded, DMA)

            def step(s, parity, nth):
                if not is_last(s):
                    diagonal(s + 1)
                sum_units(s)

            steps(pe, step)
            pe.wait_ge(weights_loaded, W_DMAS * DMA)
            pe.wait_ge(h1_pooled, PAIRS)
            pe.wait_ge(h2_pooled, PAIRS)
            for layer in range(2):
                mm = pe.matmul(acc1[0:HALVES, 0:PAIRS * TILE_B], wfc_s[:, layer, :],
                               pooled[:, layer, :, :].rearrange("p g b -> p (g b)"),
                               start=(layer == 0), stop=(layer == 1))
            mm.then_inc(final_ready, 1)


def lay_out(r_x, W1, b1, W2, b2, Wfc, bfc):
    feats, hblk = partition_features()
    order = feature_order()
    tiles = r_x.reshape(PAIRS, HALVES, TILE_B, FEAT, EMB).transpose(0, 1, 3, 2, 4)
    tiles = tiles.reshape(PAIRS, HALVES, NBLK, BLK, T)
    x = tiles[:, :, ORDER].reshape(PAIRS, HALVES, XROWS, T)

    W1 = W1.reshape(FEAT, FEAT, FEAT)[order]
    W2 = W2.reshape(FEAT, FEAT, FEAT)[order]
    w1 = np.zeros((P, C1 + 1, FEAT), W1.dtype)
    w1t = np.zeros_like(w1)
    for b in range(BLK):
        for a in range(BLK):
            i, j = feats[:, a], feats[:, BLK + b]
            use = (np.arange(P) < SPARE) | (i // BLK == j // BLK)
            c = b * BLK + a
            w1[use, c] = W1[:, i, j].T[use]
            w1t[use, c] = W1[:, j, i].T[use]
    i = np.concatenate([order, order[0::2]])
    j = np.concatenate([order, order[1::2]])
    w1[:DIAG, C1] = W1[:, i, j].T
    w1t[FEAT:DIAG, C1] = W1[:, j, i].T[FEAT:]
    w2 = np.zeros((P, C2, FEAT), W2.dtype)
    for s in range(SLOTS):
        for b in range(BLK):
            c = (s // BLK) * C1 + b * BLK + s % BLK
            w2[:, c] = W2[:, feats[:, s], hblk * BLK + b].T
    bias = np.tile(np.stack([b1[order], b2[order]], axis=1), (HALVES, 1))
    wfc = np.zeros((P, 2, HALVES), Wfc.dtype)
    for h in range(HALVES):
        wfc[h * FEAT:(h + 1) * FEAT, :, h] = Wfc[0].reshape(2, FEAT)[:, order].T
    return {"x": x, "w1": w1, "w1t": w1t, "w2": w2, "bias": bias, "wfc": wfc,
            "bfc": np.tile(bfc.reshape(1, 1), (HALVES, 1))}


def kernel(r_x, L0_rec_W1, L0_rec_b1, L0_rec_W2, L0_rec_b2, L0_rec_Wfc, L0_rec_bfc):
    import concourse.bacc as bacc
    from concourse.bass_utils import run_bass_kernel_spmd

    given = (r_x, L0_rec_W1, L0_rec_b1, L0_rec_W2, L0_rec_b2, L0_rec_Wfc, L0_rec_bfc)
    arrays = {n: np.ascontiguousarray(a) for n, a in lay_out(*map(np.asarray, given)).items()}
    nc = bacc.Bacc("TRN2", target_bir_lowering=False, num_devices=1)
    args = [nc.dram_tensor(n, a.shape, F32, kind="ExternalInput").ap() for n, a in arrays.items()]
    out = nc.dram_tensor("out", (BATCH, 1), F32, kind="ExternalOutput").ap()
    build(nc, *args, out.rearrange("(g h b) o -> h g (b o)", h=HALVES, b=TILE_B))
    result = run_bass_kernel_spmd(nc, [arrays], core_ids=[0])
    return result.results[0]["out"]
```
